# Optimizing a Trainium2 kernel written in Bass

```python
import numpy as np
import jax
import jax.numpy as jnp

def _softmax(x, axis=-1):
    return jax.nn.softmax(x, axis=axis)

def _gelu(x):
    return jax.nn.gelu(x, approximate=True)

def _silu(x):
    return jax.nn.silu(x)

def _sigmoid(x):
    return jax.nn.sigmoid(x)

def _layernorm(x, axis=-1, eps=1e-05):
    m = jnp.mean(x, axis=axis, keepdims=True)
    v = jnp.var(x, axis=axis, keepdims=True)
    return (x - m) / jnp.sqrt(v + eps)

def _scatter_add(tgt, idx, src, axis=0):
    return tgt.at[idx].add(src)

def _segment_sum(src, seg, n):
    return jax.ops.segment_sum(src, seg, n)
kernel_name = 'mk_gnn_preln_d1_gnn_r8_fb5921'

def setup_inputs(seed: int=0):
    np.random.seed(seed)
    _w = jnp.asarray

    def _rec_inputs():
        import jax
        import jax.numpy as jnp
        _gk = jax.random.key(seed)
        x = -0.0003713 + 1 * jax.random.normal(jax.random.fold_in(_gk, 1), (6250, 128), jnp.float32)
        src = jax.random.randint(jax.random.fold_in(_gk, 2), (100000,), 0, 6250, jnp.int32)
        dst = jnp.minimum((6250 * jax.random.uniform(jax.random.fold_in(_gk, 3), (100000,)) ** 2.0).astype(jnp.int32), 49999)
        _o = jnp.argsort(dst, stable=True)
        src = src[_o]
        dst = dst[_o]
        edge_type_8 = jax.random.randint(jax.random.fold_in(_gk, 12), (100000,), 0, 8, jnp.int32)
        return (x, src, dst, edge_type_8)
    x, src, dst, edge_type_8 = _rec_inputs()

    def _L0_gnn_setup():
        import jax, jax.numpy as jnp
        import numpy as np
        N_NODES = 12500
        N_EDGES = 75000
        H = 128
        T = 8
        L = 2

        def _gru_cell(x, h, wih, whh, bih, bhh):
            gi = x @ wih.T + bih
            gh = h @ whh.T + bhh
            i_r, i_z, i_n = jnp.split(gi, 3, axis=-1)
            h_r, h_z, h_n = jnp.split(gh, 3, axis=-1)
            r = jax.nn.sigmoid(i_r + h_r)
            z = jax.nn.sigmoid(i_z + h_z)
            n = jnp.tanh(i_n + r * h_n)
            return (1.0 - z) * n + z * h
        key = jax.random.key(seed)
        ks = jax.random.split(key, 12)
        s = 1.0 / np.sqrt(H)
        inp = {'node_features': jax.random.normal(ks[0], (N_NODES, H), dtype=jnp.float32), 'edge_index': jax.random.randint(ks[1], (2, N_EDGES), 0, N_NODES, dtype=jnp.int64), 'edge_type': jax.random.randint(ks[2], (N_EDGES,), 0, T, dtype=jnp.int64), 'node_proj_w': jax.random.uniform(ks[3], (H, H), jnp.float32, -s, s), 'node_proj_b': jax.random.uniform(ks[4], (H,), jnp.float32, -s, s), 'edge_W': jax.random.uniform(ks[5], (L, T, H, H), jnp.float32, -s, s), 'edge_b': jax.random.uniform(ks[6], (L, T, H), jnp.float32, -s, s), 'gru_wih': jax.random.uniform(ks[7], (L, 3 * H, H), jnp.float32, -s, s), 'gru_whh': jax.random.uniform(ks[8], (L, 3 * H, H), jnp.float32, -s, s), 'gru_bih': jax.random.uniform(ks[9], (L, 3 * H), jnp.float32, -s, s), 'gru_bhh': jax.random.uniform(ks[10], (L, 3 * H), jnp.float32, -s, s), 'out_w': jax.random.uniform(ks[11], (H, H), jnp.float32, -s, s), 'out_b': jnp.zeros((H,), jnp.float32)}
        return inp
    _L0_gnn_all = _L0_gnn_setup()
    _L0_gnn_in = {k: v for k, v in _L0_gnn_all.items() if k in ('node_proj_w', 'node_proj_b', 'edge_W', 'edge_b', 'gru_wih', 'gru_whh', 'gru_bih', 'gru_bhh', 'out_w', 'out_b')}
    del _L0_gnn_all
    return {'x': x, 'src': src, 'dst': dst, 'edge_type_8': edge_type_8, 'L0_gnn_node_proj_w': _L0_gnn_in['node_proj_w'], 'L0_gnn_node_proj_b': _L0_gnn_in['node_proj_b'], 'L0_gnn_edge_W': _L0_gnn_in['edge_W'], 'L0_gnn_edge_b': _L0_gnn_in['edge_b'], 'L0_gnn_gru_wih': _L0_gnn_in['gru_wih'], 'L0_gnn_gru_whh': _L0_gnn_in['gru_whh'], 'L0_gnn_gru_bih': _L0_gnn_in['gru_bih'], 'L0_gnn_gru_bhh': _L0_gnn_in['gru_bhh'], 'L0_gnn_out_w': _L0_gnn_in['out_w'], 'L0_gnn_out_b': _L0_gnn_in['out_b']}

def reference(x, src, dst, edge_type_8, L0_gnn_node_proj_w, L0_gnn_node_proj_b, L0_gnn_edge_W, L0_gnn_edge_b, L0_gnn_gru_wih, L0_gnn_gru_whh, L0_gnn_gru_bih, L0_gnn_gru_bhh, L0_gnn_out_w, L0_gnn_out_b):
    import jax
    import jax.numpy as jnp

    def _L0_gnn_ref(node_features, edge_index, edge_type, node_proj_w, node_proj_b, edge_W, edge_b, gru_wih, gru_whh, gru_bih, gru_bhh, out_w, out_b):
        import jax, jax.numpy as jnp
        import numpy as np
        N_NODES = 12500
        N_EDGES = 75000
        H = 128
        T = 8
        L = 2

        def _gru_cell(x, h, wih, whh, bih, bhh):
            gi = x @ wih.T + bih
            gh = h @ whh.T + bhh
            i_r, i_z, i_n = jnp.split(gi, 3, axis=-1)
            h_r, h_z, h_n = jnp.split(gh, 3, axis=-1)
            r = jax.nn.sigmoid(i_r + h_r)
            z = jax.nn.sigmoid(i_z + h_z)
            n = jnp.tanh(i_n + r * h_n)
            return (1.0 - z) * n + z * h
        num_nodes = node_features.shape[0]
        src, dst = (edge_index[0], edge_index[1])
        h = jax.nn.relu(node_features @ node_proj_w.T + node_proj_b)
        for l in range(L):
            trans = jnp.einsum('nh,tdh->tnd', h, edge_W[l])
            msgs = trans[edge_type, src]
            agg = jax.ops.segment_sum(msgs, dst, num_segments=num_nodes)
            h = _gru_cell(agg, h, gru_wih[l], gru_whh[l], gru_bih[l], gru_bhh[l])
            h = jax.nn.relu(h)
        return h @ out_w.T + out_b
    edge_index = jnp.stack([src, dst])
    h = jnp.maximum(_layernorm(x, axis=-1), 0.0)
    x = x + _L0_gnn_ref(h, edge_index, edge_type_8, L0_gnn_node_proj_w, L0_gnn_node_proj_b, L0_gnn_edge_W, L0_gnn_edge_b, L0_gnn_gru_wih, L0_gnn_gru_whh, L0_gnn_gru_bih, L0_gnn_gru_bhh, L0_gnn_out_w, L0_gnn_out_b)
    return x

_drawn_inputs = setup_inputs


def setup_inputs(seed=0):
    import zlib

    import numpy as np

    out = dict(_drawn_inputs(seed))
    spreads = {'L0_gnn_out_b': (0.0, 0.1)}
    factors = {'L0_gnn_node_proj_b': 4.541,
     'L0_gnn_gru_whh': 2.983,
     'L0_gnn_gru_bih': 4.098,
     'L0_gnn_gru_bhh': 7.314}
    for name, (base, spread) in spreads.items():
        noise = np.random.default_rng([zlib.crc32(name.encode()), seed]).standard_normal(out[name].shape)
        drawn = base * np.exp(spread * noise) if base else spread * noise
        out[name] = jnp.asarray(drawn.astype(out[name].dtype))
    for name, factor in factors.items():
        out[name] = (out[name] * factor).astype(out[name].dtype)
    return out
```

```python
from contextlib import ExitStack

import concourse.bass as bass
from concourse import mybir

F32 = mybir.dt.float32
BF16 = mybir.dt.bfloat16
I32 = mybir.dt.int32
ALU = mybir.AluOpType
ACT = mybir.ActivationFunctionType
AX = mybir.AxisListType
ds = bass.ds

H = 128
N = 6250
E = 100000
T = 8
L = 2
G3 = 3
EPS = 1e-5

GE = 128
WIN = 32
CODES = T * WIN
BG = 4
SLOTS = 4
ROUNDS = -(-E // (GE * BG * SLOTS))
BATCHES = ROUNDS * SLOTS
GROUPS = BATCHES * BG
AHEAD = SLOTS * BG
ROWP = 112
RC = GROUPS // ROWP
assert RC * ROWP == GROUPS
FULL = (RC - 1) * ROWP * GE
LAST_ROWS = (E - FULL) // GE
LAST = E - FULL - LAST_ROWS * GE
OUTSIDE = 1e6

TC = 4
TILE = ROWP * TC
TILES = -(-N // TILE)
NPAD = TILES * TILE
CHUNKS = TILES * TC
TAIL_ROWS = N - (CHUNKS - 1) * ROWP
ACCW = NPAD + WIN
assert 0 < TAIL_ROWS <= ROWP and TILES % 2 == 0 and ACCW >= N + WIN

PARTS = 3
NW = L * T + 2 * L * G3 + 2
W_EDGE, W_IH, W_HH = 0, L * T, L * T + L * G3
W_PROJ, W_OUT = NW - 2, NW - 1


def gnn_kernel(nc, x, src, dst, etype, proj_w, proj_b, edge_w, wih, whh, bih, bhh, out_w, out_b, out):
    with ExitStack() as ctx:
        def sb(name, shape, dt=F32):
            return ctx.enter_context(nc.sbuf_tensor(name, shape, dt))

        def sem(name):
            return ctx.enter_context(nc.semaphore(name))

        table = nc.dram_tensor("node_table", (NPAD, PARTS * H), BF16, kind="Internal").ap()

        x_sb = sb("x_sb", [ROWP, CHUNKS, H])
        hT = sb("hT", [H, NPAD])
        acc = sb("acc", [H, ACCW])
        w_nat = sb("w_nat", [H, NW, H])
        wT = sb("wT", [H, NW, H])
        ident = sb("ident", [128, 128])
        bias = sb("bias", [H, 16])
        brz = sb("brz", [H, L, 2])
        outb_row = sb("outb_row", [1, H])
        ones_row = sb("ones_row", [1, ROWP])
        iota_i = sb("iota_i", [128, CODES], I32)
        iota_b = sb("iota_b", [128, CODES], BF16)

        srcT = sb("srcT", [GE, GROUPS + AHEAD], I32)
        relT = sb("relT", [GE, GROUPS + AHEAD])
        typT = sb("typT", [GE, GROUPS + AHEAD])
        code = sb("code", [GE, GROUPS + AHEAD])
        code_a = sb("code_a", [GE, GROUPS + AHEAD])
        woff = sb("woff", [128, 1])
        base = sb("base", [ROWP, RC])
        top = sb("top", [ROWP, RC])
        span = sb("span", [ROWP, 1])
        base_row = sb("base_row", [1, GROUPS])
        start_row = sb("start_row", [1, GROUPS], I32)
        span_f = sb("span_f", [1, 1])
        span_i = sb("span_i", [1, 1], I32)
        passes = sb("passes", [1, 2], I32)

        gidx = sb("gidx", [GE, SLOTS, BG], I32)
        gath = sb("gath", [GE, SLOTS, BG, PARTS * H], BF16)
        onehot = sb("onehot", [GE, SLOTS, BG, CODES], BF16)
        s_sb = sb("s_sb", [H, 2, BG, CODES])

        stats = sb("stats", [ROWP, CHUNKS, 6])
        mv = sb("mv", [ROWP, CHUNKS, 2])
        rstd = sb("rstd", [ROWP, CHUNKS])
        var = sb("var", [ROWP, CHUNKS])
        dev = sb("dev", [ROWP, CHUNKS])
        nmean = sb("nmean", [ROWP, CHUNKS])
        y_sb = sb("y_sb", [ROWP, 2, TC, H])
        yT = sb("yT", [H, 2, TILE])
        rg = sb("rg", [H, 2, TILE])
        zg = sb("zg", [H, 2, TILE])
        ng = sb("ng", [H, 2, TILE])
        tg = sb("tg", [H, 2, TILE])
        h_cur = sb("h_cur", [H, 2, TILE])
        rem = sb("rem", [ROWP, 2, TC, H])
        tab_sb = sb("tab_sb", [ROWP, 2, TC, PARTS * H], BF16)

        def rows(n, dt=F32):
            return acc[0:ROWP, n * RC * GE:(n + 1) * RC * GE].bitcast(dt).rearrange("p (c e) -> p c e", c=RC)
        dst_i, src_i, typ_i = (rows(n, I32) for n in range(3))
        dst_f, src_f, typ_f, rel_f = (rows(n) for n in range(3, 7))

        ps = ctx.enter_context(nc.psum_tensor("ps", [128, 8, 512], F32))
        sums = [ps[:, 2 * b:2 * b + 2, :].rearrange("p a (g c) -> p (a g) c", c=CODES) for b in range(2)]
        win_ps = [ps[:, 4 + b, 0:BG * WIN] for b in range(2)]
        hn_ps, r_ps, z_ps, in_ps = (ps[:, b, 0:TILE] for b in range(4))
        rows_ps = [ps[0:ROWP, 4 + b, :].rearrange("p (c h) -> p c h", c=TC) for b in range(2)]
        yT_ps = ps[:, 6, 0:TILE]

        weights_in, bias_in, edges_in, tail_in = sem("weights_in"), sem("bias_in"), sem("edges_in"), sem("tail_in")
        x_in = [sem(f"x_in{q}") for q in range(4)]
        x_cleared, rows_cleared = sem("x_cleared"), sem("rows_cleared")
        ident_set, iota_set = sem("ident_set"), sem("iota_set")
        iota_ready = sem("iota_ready")
        dve_step = sem("dve_step")
        wT_ps_ready, wT_copied = sem("wT_ps_ready"), sem("wT_copied")
        rows_ready, rowsT_ready, rowsT_copied = sem("rows_ready"), sem("rowsT_ready"), sem("rowsT_copied")
        base_ready, base_ps_ready = sem("base_ready"), sem("base_ps_ready")
        passes_ready = sem("passes_ready")
        norm_ready, bias_ready = sem("norm_ready"), sem("bias_ready")
        var_ready, dev_ready = sem("var_ready"), sem("dev_ready")
        acc_cleared = sem("acc_cleared")

        stage_sems = ("y_done", "y_turned", "yT_copied", "hn_ready", "r_ready", "z_ready", "in_ready",
                      "r_done", "z_done", "t_mul", "t_add", "n_done", "d_sub", "d_mul", "d_add", "h_done", "h_kept",
                      "turned", "hi_done", "rem_done", "mid_done", "lo_done", "out_done")
        st = [{k: sem(f"{k}{s}") for k in stage_sems} for s in range(L + 1)]
        stored = [sem(f"stored{b}") for b in range(2)]
        edge_sems = ("idx_staged", "gathers_begun", "pass_gathered", "pass_begun", "hot_ready", "sums_ready", "sums_copied",
                     "win_done", "acc_added", "codes", "edges_done")
        es = [{k: sem(f"{k}{l}") for k in edge_sems} for l in range(L)]
        gathered = [[sem(f"gathered{l}_{b}") for b in range(SLOTS)] for l in range(L)]
        out_stored = [sem(f"out_stored{b}") for b in range(2)]

        block = ctx.enter_context(nc.Block())

        def tile_cols(i):
            return ds(i * TILE, TILE)

        def each_tile(eng, head, tail):
            head(0, 0)
            for i in range(2):
                head(i + 1, (i + 1) % 2)
                tail(i, i % 2)
            with eng.Fori(0, TILES // 2 - 2) as n:
                for b in range(2):
                    head(n * 2 + (b + 3), (b + 1) % 2)
                    tail(n * 2 + (b + 2), b)
            head(TILES - 1, 1)
            tail(TILES - 2, 0)
            tail(TILES - 1, 1)

        def wait_count(eng, s, count, back=0):
            if isinstance(count, int):
                if count > back:
                    eng.wait_ge(s, count - back)
            else:
                eng.wait_ge(s, count - back)

        @block.sync
        def _(sp):
            sp.dma_start(w_nat[:, W_PROJ, :], proj_w).then_inc(weights_in, 16)
            sp.dma_start(w_nat[:, W_OUT, :], out_w).then_inc(weights_in, 16)
            sp.wait_ge(rows_cleared, 3)
            for a, (arr, to) in enumerate(((dst, dst_i), (src, src_i), (etype, typ_i))):
                sp.dma_start(to[:, 0:RC - 1, :],
                             arr[0:FULL].rearrange("(c p e) -> p c e", p=ROWP, e=GE)).then_inc(edges_in, 16)
                sp.dma_start(to[0:LAST_ROWS, RC - 1, :],
                             arr[FULL:FULL + LAST_ROWS * GE].rearrange("(p e) -> p e", e=GE)).then_inc(edges_in, 16)
                for q in range(GE // LAST if a == 0 else 1):
                    sp.dma_start(to[LAST_ROWS:LAST_ROWS + 1, RC - 1, q * LAST:(q + 1) * LAST],
                                 arr[E - LAST:E].rearrange("(a e) -> a e", a=1)).then_inc(edges_in, 16)
            sp.wait_ge(x_cleared, 1)
            for q in range(4):
                lo, hi = q * CHUNKS // 4, min((q + 1) * CHUNKS // 4, CHUNKS - 1)
                sp.dma_start(x_sb[:, lo:hi, :],
                             x[lo * ROWP:hi * ROWP, :].rearrange("(c p) h -> p c h", p=ROWP)).then_inc(x_in[q], 16)
            sp.dma_start(x_sb[0:TAIL_ROWS, CHUNKS - 1, :], x[N - TAIL_ROWS:N, :]).then_inc(x_in[3], 16)
            for l in range(L):
                sp.dma_start(w_nat[:, W_EDGE + l * T:W_EDGE + (l + 1) * T, :],
                             edge_w[l].rearrange("t d h -> d t h")).then_inc(weights_in, 16)
                sp.dma_start(w_nat[:, W_IH + l * G3:W_IH + (l + 1) * G3, :],
                             wih[l].rearrange("(g d) h -> d g h", g=G3)).then_inc(weights_in, 16)
                sp.dma_start(w_nat[:, W_HH + l * G3:W_HH + (l + 1) * G3, :],
                             whh[l].rearrange("(g d) h -> d g h", g=G3)).then_inc(weights_in, 16)
            for s in range(L):
                def store(i, b):
                    sp.wait_ge(st[s]["lo_done"], i + 1)
                    sp.dma_start(table[tile_cols(i), :].rearrange("(c p) f -> p c f", p=ROWP),
                                 tab_sb[:, b]).then_inc(stored[b], 16)
                with sp.Fori(0, TILES // 2) as n:
                    for b in range(2):
                        store(n * 2 + b, b)
            def put(i, b):
                sp.wait_ge(st[L]["out_done"], i + 1)
                sp.dma_start(out[tile_cols(i), :].rearrange("(c p) h -> p c h", p=ROWP),
                             x_sb[:, ds(i * TC, TC), :]).then_inc(out_stored[b], 16)
            with sp.Fori(0, TILES // 2 - 1) as n:
                for b in range(2):
                    put(n * 2 + b, b)
            put(TILES - 2, 0)
            sp.wait_ge(st[L]["out_done"], TILES)
            sp.dma_start(out[(TILES - 1) * TILE:(CHUNKS - 1) * ROWP, :].rearrange("(c p) h -> p c h", p=ROWP),
                         x_sb[:, (TILES - 1) * TC:CHUNKS - 1, :]).then_inc(out_stored[1], 16)
            sp.dma_start(out[N - TAIL_ROWS:N, :], x_sb[0:TAIL_ROWS, CHUNKS - 1, :]).then_inc(out_stored[1], 16)
            sp.wait_ge(out_stored[0], 16 * (TILES // 2))
            sp.wait_ge(out_stored[1], 16 * (TILES // 2 + 1))

        @block.gpsimd
        def _(pool):
            nc.gpsimd.memset(ident[:], 0.0).then_inc(ident_set, 1)
            nc.gpsimd.memset(x_sb[:, CHUNKS - 1, :], 0.0).then_inc(x_cleared, 1)
            pool.wait_ge(ident_set, 1)
            nc.gpsimd.affine_select(out=ident[:], in_=ident[:], compare_op=ALU.not_equal, fill=1.0, base=0,
                                    pattern=[[-1, 128]], channel_multiplier=1).then_inc(ident_set, 1)
            nc.gpsimd.iota(iota_i[:], pattern=[[1, CODES]], base=0, channel_multiplier=0).then_inc(iota_set, 1)
            def keep_states(s):
                with pool.Fori(0, TILES // 2) as n:
                    for b in range(2):
                        i = n * 2 + b
                        pool.wait_ge(st[s]["h_done"], i + 1)
                        nc.gpsimd.tensor_copy(hT[:, tile_cols(i)], h_cur[:, b, :]).then_inc(st[s]["h_kept"], 1)

            for l in range(L):
                keep_states(l)
                if l == 0:
                    pool.wait_ge(rowsT_ready, 6)
                else:
                    pool.wait_ge(st[l]["in_ready"], TILES)
                nc.gpsimd.memset(acc[:], 0.0).then_inc(acc_cleared, 1)
                pool.wait_ge(passes_ready, 1)
                n_pass = pool.value_load(passes[0:1, 1:2], min_val=1, max_val=N)
                for b in range(2):
                    pool.wait_ge(stored[b], 16 * (TILES // 2) * (l + 1))
                with pool.Fori(0, n_pass) as p:
                    with pool.Fori(0, ROUNDS) as n:
                        for b in range(SLOTS):
                            k = p * BATCHES + n * SLOTS
                            pool.wait_ge(es[l]["idx_staged"], k + (b + 1))
                            pool.wait_ge(es[l]["sums_ready"], k + (b + 1))
                            pool.sem_inc(es[l]["gathers_begun"], 1)
                            for j in range(BG):
                                nc.gpsimd.indirect_dma_start(
                                    out=gath[:, b, j, :], out_offset=None, in_=table,
                                    in_offset=bass.IndirectOffsetOnAxis(ap=gidx[:, b, j:j + 1], axis=0),
                                ).then_inc(gathered[l][b], 16)
                    pool.wait_ge(es[l]["sums_ready"], p * BATCHES + (BATCHES + SLOTS))
                    pool.sem_inc(es[l]["pass_gathered"], 1)
                    nc.gpsimd.inc_swdge_sem(gathered[l], [ROUNDS * BG * 16] * SLOTS, mode="sub")

        @block.scalar
        def _(act):
            with nc.allow_non_contiguous_dma(reason="a few hundred words"):
                act.dma_start(bias[:, 0:1], proj_b.rearrange("(d a) -> d a", a=1)).then_inc(bias_in, 16)
                act.dma_start(bias[:, 1:1 + L * G3], bih.rearrange("l (g d) -> d (l g)", g=G3)).then_inc(bias_in, 16)
                act.dma_start(bias[:, 7:7 + L * G3], bhh.rearrange("l (g d) -> d (l g)", g=G3)).then_inc(bias_in, 16)
            act.dma_start(outb_row[:], out_b.rearrange("(a d) -> a d", a=1)).then_inc(bias_in, 16)

            def copy_wT(q):
                lo, hi = q * 4, min(q * 4 + 4, NW)
                act.wait_ge(wT_ps_ready, q + 1)
                act.copy(wT[:, lo:hi, :], ps[:, q % 4, 0:(hi - lo) * H].rearrange("p (w h) -> p w h", h=H)) \
                   .then_inc(wT_copied, 1)
            copy_wT(0)
            for q in range(1, -(-NW // 4)):
                copy_wT(q)

            def cur_free(s, i):
                if isinstance(i, int) and i < 2:
                    return
                act.wait_ge(st[s]["turned"], i - 1)
                if s < L:
                    act.wait_ge(st[s]["h_kept"], i - 1)

            def stage0_head(i, b):
                act.wait_ge(norm_ready, 1)
                if not (isinstance(i, int) and i < 2):
                    act.wait_ge(st[0]["y_turned"], i - 1)
                for c in range(TC):
                    ch = i * TC + c
                    last = act.activation(y_sb[:, b, c, :], x_sb[:, ds(ch, 1), :].rearrange("p a h -> p (a h)"),
                                          ACT.Relu, bias=nmean[:, ds(ch, 1)], scale=rstd[:, ds(ch, 1)])
                last.then_inc(st[0]["y_done"], 1)
                act.wait_ge(st[0]["in_ready"], i + 1)
                cur_free(0, i)
                act.activation(h_cur[:, b, :], in_ps, ACT.Relu, bias=bias[:, 0:1]).then_inc(st[0]["h_done"], 1)

            def gates_head(s):
                l = s - 1
                def head(i, b):
                    act.wait_ge(st[s]["r_ready"], i + 1)
                    act.activation(rg[:, b, :], r_ps, ACT.Sigmoid, bias=brz[:, l, 0:1]).then_inc(st[s]["r_done"], 1)
                    act.wait_ge(st[s]["z_ready"], i + 1)
                    act.activation(zg[:, b, :], z_ps, ACT.Sigmoid, bias=brz[:, l, 1:2]).then_inc(st[s]["z_done"], 1)
                    act.wait_ge(st[s]["t_add"], i + 1)
                    act.activation(ng[:, b, :], tg[:, b, :], ACT.Tanh, bias=bias[:, 3 + 3 * l:4 + 3 * l]) \
                       .then_inc(st[s]["n_done"], 1)
                    act.wait_ge(st[s]["d_add"], i + 1)
                    cur_free(s, i)
                    act.activation(h_cur[:, b, :], tg[:, b, :], ACT.Relu).then_inc(st[s]["h_done"], 1)
                return head

            def split_tail(s):
                def tail(i, b):
                    act.wait_ge(st[s]["turned"], i + 1)
                    if not (isinstance(i, int) and i < 2 and s == 0):
                        act.wait_ge(stored[b], (i - b) * 8 + 16 * (TILES // 2) * s)
                    act.copy(tab_sb[:, b, :, 0:H], rows_ps[b]).then_inc(st[s]["hi_done"], 1)
                    act.wait_ge(st[s]["rem_done"], i + 1)
                    act.copy(tab_sb[:, b, :, H:2 * H], rem[:, b]).then_inc(st[s]["mid_done"], 1)
                return tail

            act.wait_ge(var_ready, 1)
            act.activation(dev[:], var[:], ACT.Sqrt).then_inc(dev_ready, 1)
            act.wait_ge(bias_in, 64)
            each_tile(act, stage0_head, split_tail(0))
            act.wait_ge(passes_ready, 1)
            act.wait_ge(rowsT_copied, 7)
            act.wait_ge(bias_ready, 1)
            for l in range(L):
                n_pass = act.value_load(passes[0:1, 1:2], min_val=1, max_val=N)
                act.sem_inc(es[l]["sums_copied"], 2)

                def stage_idx(group, b):
                    act.copy(gidx[:, b, :], srcT[:, ds(group, BG)]).then_inc(es[l]["idx_staged"], 1)

                for b in range(SLOTS):
                    stage_idx(b * BG, b)
                with act.Fori(0, n_pass) as p:
                    with act.Fori(0, ROUNDS) as n:
                        for b in range(SLOTS):
                            k = p * BATCHES + n * SLOTS
                            act.wait_ge(es[l]["sums_ready"], k + (b + 1 + SLOTS))
                            act.wait_ge(es[l]["win_done"], k + (b + 1))
                            act.copy(s_sb[:, b % 2], sums[b % 2]).then_inc(es[l]["sums_copied"], 1)
                            stage_idx(n * (SLOTS * BG) + (b + SLOTS) * BG, b)
                act.wait_ge(es[l]["edges_done"], n_pass)
                each_tile(act, gates_head(l + 1), split_tail(l + 1) if l < L - 1 else lambda i, b: None)

        @block.tensor
        def _(pe):
            def turn_weights(q):
                if q >= 4:
                    pe.wait_ge(wT_copied, q - 3)
                lo, hi = q * 4, min(q * 4 + 4, NW)
                for w in range(lo, hi):
                    last = nc.tensor.transpose(ps[:, q % 4, (w - lo) * H:(w - lo + 1) * H], w_nat[:, w, :], ident[:])
                last.then_inc(wT_ps_ready, 1)

            pe.wait_ge(ident_set, 2)
            pe.wait_ge(rows_ready, 1)
            for q in range(6):
                if q >= 2:
                    pe.wait_ge(rowsT_copied, q - 1)
                lo, hi = (0, 4) if q % 2 == 0 else (4, RC)
                for c in range(lo, hi):
                    last = nc.tensor.transpose(ps[:, 4 + q % 2, (c - lo) * ROWP:(c - lo + 1) * ROWP],
                                               (src_f, rel_f, typ_f)[q // 2][:, c, :], ident[0:ROWP, 0:ROWP])
                last.then_inc(rowsT_ready, 1)
            pe.wait_ge(base_ready, 1)
            for c in range(RC):
                nc.tensor.matmul(ps[0:1, 6 + c // 4, (c % 4) * ROWP:(c % 4 + 1) * ROWP], base[:, c:c + 1],
                                 ident[0:ROWP, 0:ROWP], start=True, stop=True)
            nc.tensor.matmul(ps[0:1, 7, 3 * ROWP:4 * ROWP], span[:, 0:1], ident[0:ROWP, 0:ROWP],
                             start=True, stop=True).then_inc(base_ps_ready, 1)
            pe.wait_ge(weights_in, 16 * (2 + 3 * L))
            for q in range(-(-NW // 4)):
                turn_weights(q)
            pe.wait_ge(wT_copied, -(-NW // 4))
            pe.wait_ge(passes_ready, 1)

            def project_head(i, b):
                pe.wait_ge(st[0]["y_done"], i + 1)
                wait_count(pe, st[0]["yT_copied"], i)
                for c in range(TC):
                    last = nc.tensor.transpose(yT_ps[:, c * ROWP:(c + 1) * ROWP], y_sb[:, b, c, :],
                                               ident[0:ROWP, 0:ROWP])
                last.then_inc(st[0]["y_turned"], 1)
                wait_count(pe, st[0]["h_done"], i)
                pe.wait_ge(st[0]["yT_copied"], i + 1)
                nc.tensor.matmul(in_ps, wT[:, W_PROJ, :], yT[:, b, :], start=True, stop=True) \
                  .then_inc(st[0]["in_ready"], 1)

            def gates_head(s):
                l = s - 1

                def gate(g, to, i, part):
                    cols = tile_cols(i)
                    if "i" in part:
                        last = nc.tensor.matmul(to, wT[:, W_IH + l * G3 + g, :], acc[:, cols],
                                                start=True, stop="h" not in part)
                    if "h" in part:
                        last = nc.tensor.matmul(to, wT[:, W_HH + l * G3 + g, :], hT[:, cols],
                                                start="i" not in part, stop=True)
                    return last

                def head(i, b):
                    wait_count(pe, st[s]["r_done"], i)
                    gate(0, r_ps, i, "ih").then_inc(st[s]["r_ready"], 1)
                    wait_count(pe, st[s]["t_mul"], i)
                    gate(2, hn_ps, i, "h").then_inc(st[s]["hn_ready"], 1)
                    wait_count(pe, st[s]["t_add"], i)
                    gate(2, in_ps, i, "i").then_inc(st[s]["in_ready"], 1)
                    wait_count(pe, st[s]["z_done"], i)
                    gate(1, z_ps, i, "ih").then_inc(st[s]["z_ready"], 1)
                return head

            def turn_tail(s):
                def tail(i, b):
                    pe.wait_ge(st[s]["h_done"], i + 1)
                    if not (isinstance(i, int) and i < 2):
                        pe.wait_ge(st[s]["rem_done"], i - 1)
                    for c in range(TC):
                        last = nc.tensor.transpose(rows_ps[b][:, c, :], h_cur[:, b, c * ROWP:(c + 1) * ROWP], ident[:])
                    last.then_inc(st[s]["turned"], 1)
                return tail

            def out_tail(i, b):
                pe.wait_ge(st[L]["h_done"], i + 1)
                if not (isinstance(i, int) and i < 2):
                    pe.wait_ge(st[L]["out_done"], i - 1)
                for c in range(TC):
                    nc.tensor.matmul(rows_ps[b][:, c, :], h_cur[:, b, c * ROWP:(c + 1) * ROWP], wT[:, W_OUT, :],
                                     start=True, stop=False)
                    last = nc.tensor.matmul(rows_ps[b][:, c, :], ones_row[:], outb_row[:], start=False, stop=True)
                last.then_inc(st[L]["turned"], 1)

            each_tile(pe, project_head, turn_tail(0))
            for l in range(L):
                pe.wait_ge(st[l]["h_kept"], TILES)
                n_pass = pe.value_load(passes[0:1, 1:2], min_val=1, max_val=N)
                pe.sem_inc(es[l]["sums_ready"], SLOTS)
                pe.sem_inc(es[l]["win_done"], 2)

                def sum_by_code(p, n, b):
                    k = p * BATCHES + n * SLOTS
                    pe.wait_ge(gathered[l][b], n * (16 * BG) + 16 * BG)
                    pe.wait_ge(es[l]["hot_ready"], k + (b + 1))
                    pe.wait_ge(es[l]["sums_copied"], k + (b + 1))
                    for j in range(BG):
                        for part in range(PARTS):
                            last = nc.tensor.matmul(sums[b % 2][:, j, :], gath[:, b, j, part * H:(part + 1) * H],
                                                    onehot[:, b, j, :], start=(part == 0), stop=(part == PARTS - 1))
                    last.then_inc(es[l]["sums_ready"], 1)

                def by_type(p, n, b):
                    k = p * BATCHES + n * SLOTS
                    pe.wait_ge(es[l]["sums_copied"], k + (b + 3))
                    pe.wait_ge(es[l]["acc_added"], (k + (b + 1)) * BG)
                    for t in range(T):
                        last = nc.tensor.matmul(win_ps[b % 2].rearrange("p (g w) -> p g w", g=BG),
                                                wT[:, W_EDGE + l * T + t, :],
                                                s_sb[:, b % 2, :, t * WIN:(t + 1) * WIN],
                                                start=(t == 0), stop=(t == T - 1))
                    last.then_inc(es[l]["win_done"], 1)

                with pe.Fori(0, n_pass) as p:
                    pe.wait_ge(es[l]["gathers_begun"], p * BATCHES + 1)
                    pe.sem_inc(es[l]["pass_begun"], 1)
                    with pe.Fori(0, ROUNDS) as n:
                        sum_by_code(p, n, 0)
                        for b in range(1, SLOTS):
                            sum_by_code(p, n, b)
                            by_type(p, n, b - 1)
                        by_type(p, n, SLOTS - 1)
                pe.wait_ge(es[l]["edges_done"], n_pass)
                each_tile(pe, gates_head(l + 1), turn_tail(l + 1) if l < L - 1 else out_tail)

        @block.vector
        def _(dve):
            steps = [0]

            def step(ins):
                steps[0] += 1
                ins.then_inc(dve_step, 1)
                dve.wait_ge(dve_step, steps[0])

            nc.vector.memset(dst_i[:, RC - 1, :], 0).then_inc(rows_cleared, 1)
            nc.vector.memset(src_i[:, RC - 1, :], 0).then_inc(rows_cleared, 1)
            nc.vector.memset(typ_i[:, RC - 1, :], T).then_inc(rows_cleared, 1)
            nc.vector.memset(ones_row[:], 1.0)
            dve.wait_ge(iota_set, 1)
            nc.vector.tensor_copy(iota_b[:], iota_i[:]).then_inc(iota_ready, 1)

            dve.wait_ge(edges_in, 16 * (3 * 3 + GE // LAST - 1))
            nc.vector.tensor_copy(src_f, src_i)
            nc.vector.tensor_scalar(typ_f, typ_i, float(WIN), None, ALU.mult)
            step(nc.vector.tensor_copy(dst_f, dst_i))
            nc.vector.tensor_reduce(top[:], dst_f, AX.X, ALU.max)
            step(nc.vector.tensor_reduce(base[:], dst_f, AX.X, ALU.min))
            nc.vector.tensor_tensor(rel_f, dst_f, base[:].rearrange("p (c a) -> p c a", a=1).to_broadcast([ROWP, RC, GE]),
                                    ALU.subtract).then_inc(rows_ready, 1)
            step(nc.vector.tensor_tensor(top[:], top[:], base[:], ALU.subtract))
            nc.vector.tensor_reduce(span[:], top[:], AX.X, ALU.max).then_inc(base_ready, 1)
            for q in range(6):
                dve.wait_ge(rowsT_ready, q + 1)
                lo, hi = (0, 4 * ROWP) if q % 2 == 0 else (4 * ROWP, GROUPS)
                nc.vector.tensor_copy((srcT, relT, typT)[q // 2][:, lo:hi], ps[:, 4 + q % 2, 0:hi - lo]) \
                  .then_inc(rowsT_copied, 1)
            dve.wait_ge(rowsT_copied, 6)
            nc.vector.tensor_copy(srcT[:, GROUPS:], srcT[:, 0:AHEAD]).then_inc(rowsT_copied, 1)
            nc.vector.tensor_scalar(relT[:, GROUPS:], relT[:, 0:AHEAD], float(-WIN), None, ALU.add)
            step(nc.vector.tensor_copy(typT[:, GROUPS:], typT[:, 0:AHEAD]))
            dve.wait_ge(base_ps_ready, 1)
            nc.vector.tensor_copy(base_row[:, 0:4 * ROWP], ps[0:1, 6, 0:4 * ROWP])
            nc.vector.tensor_copy(base_row[:, 4 * ROWP:], ps[0:1, 7, 0:GROUPS - 4 * ROWP])
            step(nc.vector.tensor_reduce(span_f[:], ps[0:1, 7, 3 * ROWP:4 * ROWP], AX.X, ALU.max))
            step(nc.vector.tensor_copy(span_i[:], span_f[:]))
            step(nc.vector.tensor_scalar(passes[:, 0:1], span_i[:], WIN.bit_length() - 1, None, ALU.arith_shift_right))
            nc.vector.tensor_scalar(passes[:, 1:2], passes[:, 0:1], 1.0, None, ALU.add).then_inc(passes_ready, 1)

            for q in range(4):
                dve.wait_ge(x_in[q], 16 if q < 3 else 32)
                for c in range(q * CHUNKS // 4, (q + 1) * CHUNKS // 4):
                    last = nc.vector.bn_stats(stats[:, c, :], x_sb[:, c, :])
            step(last)
            for c in range(CHUNKS):
                last = nc.vector.bn_aggr(mv[:, c, :], stats[:, c, :])
            step(last)
            nc.vector.tensor_scalar(var[:], mv[:, :, 1], EPS, None, ALU.add).then_inc(var_ready, 1)
            dve.wait_ge(dev_ready, 1)
            step(nc.vector.reciprocal(rstd[:], dev[:]))
            step(nc.vector.tensor_tensor(dev[:], rstd[:], rstd[:], ALU.mult))
            step(nc.vector.tensor_tensor(dev[:], dev[:], var[:], ALU.mult))
            step(nc.vector.tensor_scalar(dev[:], dev[:], -0.5, 1.5, ALU.mult, ALU.add))
            step(nc.vector.tensor_tensor(rstd[:], rstd[:], dev[:], ALU.mult))
            nc.vector.scalar_tensor_tensor(out=nmean[:], in0=mv[:, :, 0], scalar=-1.0, in1=rstd[:],
                                           op0=ALU.mult, op1=ALU.mult).then_inc(norm_ready, 1)
            dve.wait_ge(bias_in, 64)
            for l in range(L):
                last = nc.vector.tensor_tensor(brz[:, l, :], bias[:, 1 + G3 * l:3 + G3 * l],
                                               bias[:, 7 + G3 * l:9 + G3 * l], ALU.add)
            last.then_inc(bias_ready, 1)

            def copy_head(i, b):
                dve.wait_ge(st[0]["y_turned"], i + 1)
                if not (isinstance(i, int) and i < 2):
                    dve.wait_ge(st[0]["in_ready"], i - 1)
                nc.vector.tensor_copy(yT[:, b, :], yT_ps).then_inc(st[0]["yT_copied"], 1)

            def gates_head(s):
                l = s - 1

                def head(i, b):
                    dve.wait_ge(st[s]["hn_ready"], i + 1)
                    dve.wait_ge(st[s]["r_done"], i + 1)
                    if not (isinstance(i, int) and i < 2):
                        dve.wait_ge(st[s]["h_done"], i - 1)
                    nc.vector.scalar_tensor_tensor(out=tg[:, b, :], in0=hn_ps, scalar=bias[:, 9 + G3 * l:10 + G3 * l],
                                                   in1=rg[:, b, :], op0=ALU.add, op1=ALU.mult).then_inc(st[s]["t_mul"], 1)
                    dve.wait_ge(st[s]["in_ready"], i + 1)
                    dve.wait_ge(st[s]["t_mul"], i + 1)
                    nc.vector.tensor_tensor(tg[:, b, :], in_ps, tg[:, b, :], ALU.add).then_inc(st[s]["t_add"], 1)
                    dve.wait_ge(st[s]["n_done"], i + 1)
                    nc.vector.tensor_tensor(tg[:, b, :], hT[:, tile_cols(i)], ng[:, b, :], ALU.subtract) \
                      .then_inc(st[s]["d_sub"], 1)
                    dve.wait_ge(st[s]["z_done"], i + 1)
                    dve.wait_ge(st[s]["d_sub"], i + 1)
                    nc.vector.tensor_tensor(tg[:, b, :], tg[:, b, :], zg[:, b, :], ALU.mult).then_inc(st[s]["d_mul"], 1)
                    dve.wait_ge(st[s]["d_mul"], i + 1)
                    nc.vector.tensor_tensor(tg[:, b, :], tg[:, b, :], ng[:, b, :], ALU.add).then_inc(st[s]["d_add"], 1)
                return head

            def split_tail(s):
                def tail(i, b):
                    dve.wait_ge(st[s]["hi_done"], i + 1)
                    nc.vector.tensor_tensor(rem[:, b], rows_ps[b], tab_sb[:, b, :, 0:H], ALU.subtract) \
                      .then_inc(st[s]["rem_done"], 1)
                    dve.wait_ge(st[s]["mid_done"], i + 1)
                    nc.vector.tensor_tensor(tab_sb[:, b, :, 2 * H:3 * H], rem[:, b], tab_sb[:, b, :, H:2 * H],
                                            ALU.subtract).then_inc(st[s]["lo_done"], 1)
                return tail

            def out_tail(i, b):
                dve.wait_ge(st[L]["turned"], i + 1)
                xt = x_sb[:, ds(i * TC, TC), :]
                nc.vector.tensor_tensor(xt, rows_ps[b], xt, ALU.add).then_inc(st[L]["out_done"], 1)

            each_tile(dve, copy_head, split_tail(0))
            dve.wait_ge(iota_ready, 1)
            for l in range(L):
                sem_l = es[l]
                dve.wait_ge(st[l]["h_kept"], TILES)
                n_pass = dve.value_load(passes[0:1, 1:2], min_val=1, max_val=N)
                dve.wait_ge(acc_cleared, l + 1)
                dve.sem_inc(sem_l["acc_added"], 2 * BG)

                def one_hots(group, b):
                    for j in range(BG):
                        last = nc.vector.tensor_scalar(onehot[:, b, j, :], iota_b[:], code[:, ds(group + j, 1)], None,
                                                       ALU.is_equal)
                    last.then_inc(sem_l["hot_ready"], 1)

                CODE_STEPS = 8

                def codes(before):
                    done = [0]

                    def code_step(ins):
                        done[0] += 1
                        ins.then_inc(sem_l["codes"], 1)
                        dve.wait_ge(sem_l["codes"], before + done[0])
                    code_step(nc.vector.tensor_scalar(start_row[:], base_row[:], woff[0:1, 0:1], float(N),
                                                      ALU.subtract, ALU.min))
                    code_step(nc.vector.tensor_scalar(code[:], relT[:], woff[:, 0:1], None, ALU.add))
                    code_step(nc.vector.tensor_scalar(code_a[:], code[:], 0.0, OUTSIDE, ALU.is_lt, ALU.mult))
                    code_step(nc.vector.tensor_tensor(code_a[:], code_a[:], code[:], ALU.add))
                    code_step(nc.vector.tensor_tensor(code_a[:], code_a[:], typT[:], ALU.add))
                    code_step(nc.vector.tensor_scalar(code[:], code[:], float(WIN), OUTSIDE, ALU.is_ge, ALU.mult))
                    code_step(nc.vector.tensor_tensor(code[:], code[:], code_a[:], ALU.add))
                    code_step(nc.vector.tensor_scalar(woff[:], woff[:], float(-WIN), None, ALU.add))
                    assert done[0] == CODE_STEPS

                step(nc.vector.memset(woff[:], 0.0))
                codes(0)
                for b in range(SLOTS):
                    one_hots(b * BG, b)
                with dve.Fori(0, n_pass) as p:
                    with dve.Fori(0, ROUNDS) as n:
                        for b in range(SLOTS):
                            k = p * BATCHES + n * SLOTS
                            ka = k * BG
                            g0 = n * (SLOTS * BG) + b * BG
                            _, starts = nc.values_load_multi_w_load_instructions(
                                start_row[0:1, ds(g0, BG)], engines=(mybir.EngineType.DVE,), min_val=0, max_val=N,
                                skip_runtime_bounds_check_because="start_row is clamped to N, and nodes are not negative")
                            dve.wait_ge(sem_l["win_done"], k + (b + 3))
                            for j in range(BG):
                                win = acc[:, ds(starts[j], WIN)]
                                dve.wait_ge(sem_l["acc_added"], ka + ((b + 2) * BG + j))
                                last = nc.vector.tensor_tensor(win, win_ps[b % 2][:, j * WIN:(j + 1) * WIN], win, ALU.add)
                                last.then_inc(sem_l["acc_added"], 1)
                            one_hots(g0 + SLOTS * BG, b)
                    dve.wait_ge(sem_l["acc_added"], (p * BATCHES + (BATCHES + 2)) * BG)
                    dve.sem_inc(sem_l["edges_done"], 1)
                    codes(p * CODE_STEPS + CODE_STEPS)
                each_tile(dve, gates_head(l + 1), split_tail(l + 1) if l < L - 1 else out_tail)


_INS = ['x', 'src', 'dst', 'edge_type_8', 'L0_gnn_node_proj_w', 'L0_gnn_node_proj_b', 'L0_gnn_edge_W',
        'L0_gnn_gru_wih', 'L0_gnn_gru_whh', 'L0_gnn_gru_bih', 'L0_gnn_gru_bhh', 'L0_gnn_out_w', 'L0_gnn_out_b']


def kernel(**inputs):
    import numpy as _np
    import concourse.bacc as _bacc
    from concourse import mybir as _mybir
    from concourse.bass_utils import run_bass_kernel_spmd as _run

    nc = _bacc.Bacc("TRN2", target_bir_lowering=False, num_devices=1)
    arrays, args = {}, []
    for name in _INS:
        a = _np.ascontiguousarray(inputs[name])
        arrays[f"in_{name}_dram"] = a
        args.append(nc.dram_tensor(f"in_{name}_dram", a.shape, _mybir.dt.from_np(a.dtype), kind="ExternalInput").ap())
    args.append(nc.dram_tensor("out_0_dram", (N, H), F32, kind="ExternalOutput").ap())
    gnn_kernel(nc, *args)
    r = _run(nc, [arrays], core_ids=[0])
    return r.results[0]["out_0_dram"]
```
